# Optimizing a Trainium2 kernel written in Bass

```python
import numpy as np
import jax
import jax.numpy as jnp

def _softmax(x, axis=-1):
    return jax.nn.softmax(x, axis=axis)

def _gelu(x):
    return jax.nn.gelu(x, approximate=True)

def _silu(x):
    return jax.nn.silu(x)

def _sigmoid(x):
    return jax.nn.sigmoid(x)

def _layernorm(x, axis=-1, eps=1e-05):
    m = jnp.mean(x, axis=axis, keepdims=True)
    v = jnp.var(x, axis=axis, keepdims=True)
    return (x - m) / jnp.sqrt(v + eps)

def _scatter_add(tgt, idx, src, axis=0):
    return tgt.at[idx].add(src)

def _segment_sum(src, seg, n):
    return jax.ops.segment_sum(src, seg, n)
kernel_name = 'mk_rec_standalone_d1_rec_r8_53af29'

def setup_inputs(seed: int=0):
    np.random.seed(seed)
    _w = jnp.asarray

    def _rec_inputs():
        import jax
        import jax.numpy as jnp
        _rk = jax.random.key(seed)
        r_visual = 0.000121155 + 1.00018 * jax.random.normal(jax.random.fold_in(_rk, 1), (512, 256), jnp.float32)
        r_user_id = jax.random.randint(jax.random.fold_in(_rk, 2), (512,), 79, 999919, jnp.int32)
        r_hour = jax.random.randint(jax.random.fold_in(_rk, 3), (512,), 0, 24, jnp.int32)
        r_scale = jax.random.uniform(jax.random.fold_in(_rk, 4), (512, 1), jnp.float32, 0.0, 0.999884)
        r_gender = jax.random.randint(jax.random.fold_in(_rk, 5), (512,), 0, 2, jnp.int32)
        r_age = jax.random.randint(jax.random.fold_in(_rk, 6), (512,), 0, 8, jnp.int32)
        r_attribute = jax.random.randint(jax.random.fold_in(_rk, 7), (512,), 0, 40, jnp.int32)
        return (r_visual, r_user_id, r_hour, r_scale, r_gender, r_age, r_attribute)
    r_visual, r_user_id, r_hour, r_scale, r_gender, r_age, r_attribute = _rec_inputs()

    def _L0_rec_setup():
        import jax, jax.numpy as jnp
        import numpy as np
        NUM_USERS = 125000
        NUM_AGES = 8
        NUM_ATTR = 40
        FACE_K = 64
        VISUAL_DIM = 256
        HIDDEN = 512
        BATCH = 2048
        VOCAB = NUM_USERS + 24 + 2 + NUM_AGES + NUM_ATTR
        key = jax.random.key(seed)
        ks = jax.random.split(key, 24)
        s = 0.02
        inp = {'user_id': jax.random.randint(ks[0], (BATCH,), 0, NUM_USERS), 'hour': jax.random.randint(ks[1], (BATCH,), 0, 24), 'visual': jax.random.normal(ks[2], (BATCH, VISUAL_DIM), jnp.float32), 'scale': jax.random.uniform(ks[3], (BATCH, 1), jnp.float32), 'gender': jax.random.randint(ks[4], (BATCH,), 0, 2), 'age': jax.random.randint(ks[5], (BATCH,), 0, NUM_AGES), 'attribute': jax.random.randint(ks[6], (BATCH,), 0, NUM_ATTR), 'user_emb': jax.random.normal(ks[7], (NUM_USERS, FACE_K), jnp.float32) * s, 'hour_emb': jax.random.normal(ks[8], (24, FACE_K), jnp.float32) * s, 'gender_emb': jax.random.normal(ks[9], (2, FACE_K), jnp.float32) * s, 'age_emb': jax.random.normal(ks[10], (NUM_AGES, FACE_K), jnp.float32) * s, 'attr_emb': jax.random.normal(ks[11], (NUM_ATTR, FACE_K), jnp.float32) * s, 'visu_w': jax.random.normal(ks[12], (FACE_K, VISUAL_DIM), jnp.float32) * s, 'visu_b': jnp.zeros((FACE_K,), jnp.float32), 'fm_w': jax.random.normal(ks[13], (2, VOCAB), jnp.float32) * s, 'fm_b': jnp.zeros((2,), jnp.float32), 'w1': jax.random.normal(ks[14], (HIDDEN, 6 * FACE_K), jnp.float32) * s, 'b1': jnp.zeros((HIDDEN,), jnp.float32), 'w2': jax.random.normal(ks[15], (HIDDEN, HIDDEN), jnp.float32) * s, 'b2': jnp.zeros((HIDDEN,), jnp.float32), 'w3': jax.random.normal(ks[16], (2, HIDDEN), jnp.float32) * s, 'b3': jnp.zeros((2,), jnp.float32)}
        return inp
    _L0_rec_all = _L0_rec_setup()
    _L0_rec_in = {k: v for k, v in _L0_rec_all.items() if k in ('user_emb', 'hour_emb', 'gender_emb', 'age_emb', 'attr_emb', 'visu_w', 'visu_b', 'fm_w', 'fm_b', 'w1', 'b1', 'w2', 'b2', 'w3', 'b3')}
    del _L0_rec_all
    return {'r_visual': r_visual, 'r_user_id': r_user_id, 'r_hour': r_hour, 'r_scale': r_scale, 'r_gender': r_gender, 'r_age': r_age, 'r_attribute': r_attribute, 'L0_rec_user_emb': _L0_rec_in['user_emb'], 'L0_rec_hour_emb': _L0_rec_in['hour_emb'], 'L0_rec_gender_emb': _L0_rec_in['gender_emb'], 'L0_rec_age_emb': _L0_rec_in['age_emb'], 'L0_rec_attr_emb': _L0_rec_in['attr_emb'], 'L0_rec_visu_w': _L0_rec_in['visu_w'], 'L0_rec_visu_b': _L0_rec_in['visu_b'], 'L0_rec_fm_w': _L0_rec_in['fm_w'], 'L0_rec_fm_b': _L0_rec_in['fm_b'], 'L0_rec_w1': _L0_rec_in['w1'], 'L0_rec_b1': _L0_rec_in['b1'], 'L0_rec_w2': _L0_rec_in['w2'], 'L0_rec_b2': _L0_rec_in['b2'], 'L0_rec_w3': _L0_rec_in['w3'], 'L0_rec_b3': _L0_rec_in['b3']}

def reference(r_visual, r_user_id, r_hour, r_scale, r_gender, r_age, r_attribute, L0_rec_user_emb, L0_rec_hour_emb, L0_rec_gender_emb, L0_rec_age_emb, L0_rec_attr_emb, L0_rec_visu_w, L0_rec_visu_b, L0_rec_fm_w, L0_rec_fm_b, L0_rec_w1, L0_rec_b1, L0_rec_w2, L0_rec_b2, L0_rec_w3, L0_rec_b3):
    import jax
    import jax.numpy as jnp

    def _L0_rec_ref(user_id, hour, visual, scale, gender, age, attribute, user_emb, hour_emb, gender_emb, age_emb, attr_emb, visu_w, visu_b, fm_w, fm_b, w1, b1, w2, b2, w3, b3):
        import jax, jax.numpy as jnp
        import numpy as np
        NUM_USERS = 125000
        NUM_AGES = 8
        NUM_ATTR = 40
        FACE_K = 64
        VISUAL_DIM = 256
        HIDDEN = 512
        BATCH = 2048
        VOCAB = NUM_USERS + 24 + 2 + NUM_AGES + NUM_ATTR
        B = user_id.shape[0]
        cols = jnp.stack([user_id, NUM_USERS + hour, NUM_USERS + 24 + gender, NUM_USERS + 24 + 2 + age, NUM_USERS + 24 + 2 + NUM_AGES + attribute], axis=1)
        linear_part = fm_w[:, cols].sum(axis=2).T + fm_b
        user = user_emb[user_id]
        hr = hour_emb[hour]
        face = jnp.stack([gender_emb[gender], attr_emb[attribute], age_emb[age]], axis=1)
        face = scale[:, None, :] * jnp.tanh(face)
        embeddings = jnp.concatenate([user[:, None, :], hr[:, None, :], face], axis=1)
        so = jnp.square(embeddings.sum(axis=1)) - jnp.square(embeddings).sum(axis=1)
        second_order = 0.5 * so.sum(axis=1)
        fm = linear_part + second_order[:, None]
        vis = visual @ visu_w.T + visu_b
        x = jnp.concatenate([embeddings.reshape(B, 5 * FACE_K), vis], axis=1)
        x = jax.nn.relu(x @ w1.T + b1)
        x = jax.nn.relu(x @ w2.T + b2)
        x = x @ w3.T + b3
        return jax.nn.softmax(fm + x, axis=1)
    y = _L0_rec_ref(r_user_id, r_hour, r_visual, r_scale, r_gender, r_age, r_attribute, L0_rec_user_emb, L0_rec_hour_emb, L0_rec_gender_emb, L0_rec_age_emb, L0_rec_attr_emb, L0_rec_visu_w, L0_rec_visu_b, L0_rec_fm_w, L0_rec_fm_b, L0_rec_w1, L0_rec_b1, L0_rec_w2, L0_rec_b2, L0_rec_w3, L0_rec_b3)
    return y

_drawn_inputs = setup_inputs


def setup_inputs(seed=0):
    import zlib

    import numpy as np

    out = dict(_drawn_inputs(seed))
    spreads = {'L0_rec_visu_b': (0.0, 0.8),
     'L0_rec_fm_b': (0.0, 0.689),
     'L0_rec_b1': (0.0, 0.8),
     'L0_rec_b2': (0.0, 2.0),
     'L0_rec_b3': (0.0, 0.722)}
    factors = {'r_visual': 8.0,
     'r_scale': 8.0,
     'L0_rec_user_emb': 25.544,
     'L0_rec_hour_emb': 25.236,
     'L0_rec_gender_emb': 8.0,
     'L0_rec_age_emb': 8.0,
     'L0_rec_attr_emb': 8.0,
     'L0_rec_visu_w': 8.0,
     'L0_rec_w1': 8.0,
     'L0_rec_w2': 8.0,
     'L0_rec_fm_w': 8.0}
    for name, (base, spread) in spreads.items():
        noise = np.random.default_rng([zlib.crc32(name.encode()), seed]).standard_normal(out[name].shape)
        drawn = base * np.exp(spread * noise) if base else spread * noise
        out[name] = jnp.asarray(drawn.astype(out[name].dtype))
    for name, factor in factors.items():
        out[name] = (out[name] * factor).astype(out[name].dtype)
    return out
```

```python
import concourse.bass as bass
from concourse import mybir
from contextlib import ExitStack

F32 = mybir.dt.float32
F32R = mybir.dt.float32r
I32 = mybir.dt.int32
ALU = mybir.AluOpType
ACT = mybir.ActivationFunctionType
AX = mybir.AxisListType

P = 128
BATCH = 512
T = BATCH // P
K = 64
USERS = 125000
GENDER, AGE, ATTR, HOUR = (2, 0, 24), (8, 2, 26), (40, 10, 34), (24, 64, 0)
SMALL = (GENDER, AGE, ATTR, HOUR)
FACE = 50
HOUR0 = 64
SLOTS = HOUR0 + 24
VOCAB = USERS + 24 + 2 + 8 + 40
FIELDS = 5
HID = 512
KT = HID // P
VT = 256 // P


def build_rec(nc, ids, scale, visT, visuwT, visu_b, w1a, w1g, w2T, b1, b2, w3, b3, fm_b,
              hourT, genderT, ageT, attrT, face_rows, hour_rows, user_emb, fmT, out):
    ctx = ExitStack()
    with ctx:
        def sb(name, shape, dt=F32):
            return ctx.enter_context(nc.sbuf_tensor(name, shape, dt))

        def sem(name):
            return ctx.enter_context(nc.semaphore(name))

        ids_sb = sb("ids_sb", [P, FIELDS, T], I32)
        scale_sb = sb("scale_sb", [P, T])
        vis_sb = sb("vis_sb", [P, VT, BATCH])
        visuw_sb = sb("visuw_sb", [P, VT, K])
        visub_sb = sb("visub_sb", [P, 1])
        w1a_sb = sb("w1a_sb", [P, HID])
        w1g_sb = sb("w1g_sb", [P, 2, HID])
        w2_sb = sb("w2_sb", [P, KT, HID])
        b1_sb = sb("b1_sb", [1, HID])
        b2_sb = sb("b2_sb", [33, HID])
        w3_sb = sb("w3_sb", [P, 2, HID])
        b3_sb = sb("b3_sb", [P, 2])
        fmb_sb = sb("fmb_sb", [P, 2])
        tabT = sb("tabT", [P, 2, SLOTS])
        tab = sb("tab", [SLOTS, K + 2])
        user = sb("user", [P, T, K])
        fm_rows = sb("fm_rows", [P, FIELDS, T, 2])
        ident = sb("ident", [P, P])
        row_no = sb("row_no", [P, 40], I32)
        n_rows = sb("n_rows", [P, 4, T])
        last_row = sb("last_row", [P, 4, T])
        fm_off = sb("fm_off", [P, FIELDS, T])
        hour_ones = sb("hour_ones", [1, SLOTS])
        ones = sb("ones", [33, P], F32)
        ones_r = sb("ones_r", [33, P], F32R)
        u_neg = sb("u_neg", [P, T])
        u_wrap = sb("u_wrap", [P, T])
        u_row = sb("u_row", [P, T], I32)
        c_col = sb("c_col", [P, FIELDS, T])
        c_neg = sb("c_neg", [P, FIELDS, T])
        c_wrap = sb("c_wrap", [P, FIELDS, T])
        fm_col = sb("fm_col", [P, FIELDS, T], I32)
        s_neg = sb("s_neg", [P, 4, T])
        s_wrap = sb("s_wrap", [P, 4, T])
        s_row = sb("s_row", [P, 4, T])
        scale_h = sb("scale_h", [P, T], F32R)
        scale_l = sb("scale_l", [P, T])
        hot = sb("hot", [P, T, FACE])
        hot_h = sb("hot_h", [P, T, SLOTS])
        hot_l = sb("hot_l", [P, T, FACE])
        hotT_h = sb("hotT_h", [SLOTS, BATCH], F32R)
        hotT_l = sb("hotT_l", [FACE, BATCH], F32R)
        g_h = sb("g_h", [SLOTS, HID], F32R)
        g_l = sb("g_l", [SLOTS, HID], F32R)
        w1a_h = sb("w1a_h", [P, HID], F32R)
        w1a_l = sb("w1a_l", [P, HID], F32R)
        w2_h = sb("w2_h", [P, KT, HID], F32R)
        w2_l = sb("w2_l", [P, KT, HID], F32R)
        b2_r = sb("b2_r", [33, HID], F32R)
        xa_h = sb("xa_h", [P, BATCH], F32R)
        xa_l = sb("xa_l", [P, BATCH], F32R)
        h1_h = sb("h1_h", [P, KT, BATCH], F32R)
        h1_l = sb("h1_l", [P, KT, BATCH], F32R)
        sq_junk = sb("sq_junk", [SLOTS, K])
        esum = sb("esum", [P, T, K])
        esum2 = sb("esum2", [P, T, K])
        user2 = sb("user2", [P, T, K])
        sdiff = sb("sdiff", [P, T, K])
        sred = sb("sred", [P, T])
        fsq = sb("fsq", [P, T])
        fsq2 = sb("fsq2", [P, T])
        second = sb("second", [P, T])
        lin = sb("lin", [P, T, 2])
        bias2 = sb("bias2", [P, 2])
        base = sb("base", [P, T, 2])
        base2 = sb("base2", [P, T, 2])
        prod = sb("prod", [P, 2, 2, HID])
        x3 = sb("x3", [P, T, 2])
        logit = sb("logit", [P, T, 2])
        top = sb("top", [P, T])
        shifted = sb("shifted", [P, T, 2])
        expd = sb("expd", [P, T, 2])
        esm = sb("esm", [P, T])
        rsm = sb("rsm", [P, T])
        prob = sb("prob", [P, T, 2])

        bank = [ctx.enter_context(nc.psum_tensor(f"bank{i}", [P, 512], F32)) for i in range(8)]
        p_z = bank[0:4]
        p_hot_h, p_hot_l, p_fm, p_vis, p_g, p_user = bank[0], bank[1], bank[3], bank[4], bank[5], bank[6]
        p_h1 = [bank[7], bank[4], bank[5], bank[6]]
        fm = p_fm[:, 0:T * (K + 2)].rearrange("p (t k) -> p t k", t=T)

        ld_ids, ld_scale, ld_tabT, ld_tab = sem("ld_ids"), sem("ld_scale"), sem("ld_tabT"), sem("ld_tab")
        ld_w1g, ld_vis, ld_visuw, ld_w1a = sem("ld_w1g"), sem("ld_vis"), sem("ld_visuw"), sem("ld_w1a")
        ld_w2 = [sem(f"ld_w2_{k}") for k in range(KT)]
        ld_b1, ld_b2, ld_w3, ld_bias, ld_visub = sem("ld_b1"), sem("ld_b2"), sem("ld_w3"), sem("ld_bias"), sem("ld_visub")
        got_user = [sem(f"got_user{t}") for t in range(T)]
        got_fm = sem("got_fm")
        st_out = sem("st_out")
        tab_zero, sizes_set, pool_const, hot_zero, b2_zero, ones_set = (
            sem("tab_zero"), sem("sizes_set"), sem("pool_const"), sem("hot_zero"), sem("b2_zero"), sem("ones_set"))
        u_step, c_step, s_step = sem("u_step"), sem("c_step"), sem("s_step")
        scale_split, hot_made, hot_scaled = sem("scale_split"), sem("hot_made"), sem("hot_scaled")
        hot_on_slots, hotT_copied = sem("hot_on_slots"), sem("hotT_copied")
        tabT_tanh, tab_tanh, tab_ready = sem("tabT_tanh"), sem("tab_tanh"), sem("tab_ready")
        g_done, gh_made, gl_made = sem("g_done"), sem("gh_made"), sem("gl_made")
        vis_done, vish_made, visl_made = sem("vis_done"), sem("vish_made"), sem("visl_made")
        user_done, userh_made, userl_made = sem("user_done"), sem("userh_made"), sem("userl_made")
        w1h_made, w1l_made, w2h_made, w2l_made = sem("w1h_made"), sem("w1l_made"), sem("w2h_made"), sem("w2l_made")
        b2_split = sem("b2_split")
        h1_done, h1h_made, h1l_made = sem("h1_done"), sem("h1h_made"), sem("h1l_made")
        z_done, x3_made = sem("z_done"), sem("x3_made")
        fm_done, fm_read, sumsq, second_made, base_step = (
            sem("fm_done"), sem("fm_read"), sem("sumsq"), sem("second_made"), sem("base_step"))
        user2_made = sem("user2_made")
        soft, exp_made = sem("soft"), sem("exp_made")

        block = ctx.enter_context(nc.Block())

        @block.sync
        def _(sp):
            sp.dma_start(ids_sb[:, :, :], ids).then_inc(ld_ids, 16)
            sp.dma_start(scale_sb[:, :], scale).then_inc(ld_scale, 16)
            sp.dma_start(w1g_sb[:, :, :], w1g).then_inc(ld_w1g, 16)
            sp.dma_start(vis_sb[:, :, :], visT).then_inc(ld_vis, 16)
            sp.dma_start(w1a_sb[:, :], w1a).then_inc(ld_w1a, 16)
            for k in range(KT):
                sp.dma_start(w2_sb[:, k, :], w2T[k]).then_inc(ld_w2[k], 16)
            sp.dma_start(w3_sb[:, :, :], w3.partition_broadcast(P)).then_inc(ld_w3, 16)
            sp.dma_start(b3_sb[:, :], b3.partition_broadcast(P)).then_inc(ld_bias, 16)
            sp.dma_start(fmb_sb[:, :], fm_b.partition_broadcast(P)).then_inc(ld_bias, 16)
            sp.wait_ge(soft, 6)
            sp.dma_start(out, prob[:, :, :]).then_inc(st_out, 16)
            sp.wait_ge(st_out, 16)

        @block.gpsimd
        def _(pool):
            nc.gpsimd.memset(ident[:, :], 0.0).then_inc(pool_const, 1)
            nc.gpsimd.iota(row_no[:, :], [[1, 40]], base=0, channel_multiplier=0).then_inc(pool_const, 1)
            pool.wait_ge(pool_const, 2)
            nc.gpsimd.affine_select(out=ident[:, :], in_=ident[:, :], compare_op=ALU.not_equal, fill=1.0,
                                    base=0, pattern=[[-1, P]], channel_multiplier=1).then_inc(pool_const, 1)
            pool.wait_ge(u_step, 3)
            for t in range(T):
                nc.gpsimd.indirect_dma_start(user[:, t, :], None, user_emb,
                                             bass.IndirectOffsetOnAxis(ap=u_row[:, t:t + 1], axis=0)
                                             ).then_inc(got_user[t], 16)
            pool.wait_ge(c_step, 4)
            for f in range(FIELDS):
                for t in range(T):
                    nc.gpsimd.indirect_dma_start(fm_rows[:, f, t, :], None, fmT,
                                                 bass.IndirectOffsetOnAxis(ap=fm_col[:, f, t:t + 1], axis=0)
                                                 ).then_inc(got_fm, 16)

        @block.scalar
        def _(act):
            act.wait_ge(tab_zero, 2)
            act.dma_start(tabT[0:K, 0, HOUR0:SLOTS], hourT).then_inc(ld_tabT, 16)
            act.dma_start(tabT[K:P, 0, 0:2], genderT).then_inc(ld_tabT, 16)
            act.dma_start(tabT[0:K, 1, 10:50], attrT).then_inc(ld_tabT, 16)
            act.dma_start(tabT[K:P, 1, 2:10], ageT).then_inc(ld_tabT, 16)
            act.dma_start(tab[0:FACE, 0:K], face_rows).then_inc(ld_tab, 16)
            act.dma_start(tab[HOUR0:SLOTS, 0:K], hour_rows).then_inc(ld_tab, 16)
            act.dma_start(b1_sb[:, :], b1).then_inc(ld_b1, 16)
            act.dma_start(visuw_sb[:, :, :], visuwT).then_inc(ld_visuw, 16)
            act.dma_start(visub_sb[K:P, :], visu_b).then_inc(ld_visub, 16)
            act.wait_ge(b2_zero, 1)
            act.dma_start(b2_sb[0:1, :], b2).then_inc(ld_b2, 16)
            act.dma_start(b2_sb[32:33, :], b2).then_inc(ld_b2, 16)
            act.wait_ge(ld_tabT, 64)
            nc.scalar.activation(tabT[:, :, 0:FACE], tabT[:, :, 0:FACE], ACT.Tanh).then_inc(tabT_tanh, 1)
            act.wait_ge(ld_tab, 32)
            nc.scalar.activation(tab[0:FACE, 0:K], tab[0:FACE, 0:K], ACT.Tanh).then_inc(tab_tanh, 1)
            act.wait_ge(tab_tanh, 1)
            nc.scalar.activation(sq_junk[0:FACE, :], tab[0:FACE, 0:K], ACT.Square,
                                 accum_out=tab[0:FACE, K + 1:K + 2]).then_inc(tab_ready, 1)
            nc.scalar.activation(sq_junk[HOUR0:SLOTS, :], tab[HOUR0:SLOTS, 0:K], ACT.Square,
                                 accum_out=tab[HOUR0:SLOTS, K:K + 1]).then_inc(tab_ready, 1)
            act.wait_ge(hot_on_slots, 1)
            nc.scalar.activation(hotT_h[:, :], p_hot_h[0:SLOTS, :], ACT.Copy).then_inc(hotT_copied, 1)
            act.wait_ge(hot_on_slots, 2)
            nc.scalar.activation(hotT_l[:, :], p_hot_l[0:FACE, :], ACT.Copy).then_inc(hotT_copied, 1)
            act.wait_ge(g_done, 1)
            nc.scalar.activation(g_h[:, :], p_g[0:SLOTS, :], ACT.Copy).then_inc(gh_made, 1)
            act.wait_ge(ld_visub, 16)
            act.wait_ge(vis_done, 1)
            nc.scalar.activation(xa_h[K:P, :], p_vis[K:P, :], ACT.Identity, bias=visub_sb[K:P, :]).then_inc(vish_made, 1)
            act.wait_ge(ld_w1a, 16)
            nc.scalar.activation(w1a_h[:, :], w1a_sb[:, :], ACT.Copy).then_inc(w1h_made, 1)
            for k in range(2):
                act.wait_ge(ld_w2[k], 16)
                nc.scalar.activation(w2_h[:, k, :], w2_sb[:, k, :], ACT.Copy).then_inc(w2h_made, 1)
            act.wait_ge(user_done, 1)
            nc.scalar.activation(xa_h[0:K, :], p_user[0:K, :], ACT.Copy).then_inc(userh_made, 1)
            for k in range(2, KT):
                act.wait_ge(ld_w2[k], 16)
                nc.scalar.activation(w2_h[:, k, :], w2_sb[:, k, :], ACT.Copy).then_inc(w2h_made, 1)
            for m in range(KT):
                act.wait_ge(h1_done, m + 1)
                nc.scalar.activation(h1_h[:, m, :], p_h1[m][:, :], ACT.Relu).then_inc(h1h_made, 1)
            act.wait_ge(soft, 3)
            nc.scalar.activation(expd[:, :, :], shifted[:, :, :], ACT.Exp).then_inc(exp_made, 1)

        @block.vector
        def _(dve):
            nc.vector.memset(tabT[:, :, :], 0.0).then_inc(tab_zero, 1)
            nc.vector.memset(tab[:, :], 0.0).then_inc(tab_zero, 1)
            nc.vector.memset(b2_sb[:, :], 0.0).then_inc(b2_zero, 1)
            for f, (rows, _, _) in enumerate(SMALL):
                nc.vector.memset(n_rows[:, f, :], float(rows)).then_inc(sizes_set, 1)
                nc.vector.memset(last_row[:, f, :], float(rows - 1)).then_inc(sizes_set, 1)
            nc.vector.memset(fm_off[:, 0, :], 0.0).then_inc(sizes_set, 1)
            for f, (_, _, col) in enumerate(SMALL):
                nc.vector.memset(fm_off[:, f + 1, :], float(USERS + col)).then_inc(sizes_set, 1)
            nc.vector.memset(hot_h[:, :, :], 0.0).then_inc(hot_zero, 1)
            dve.wait_ge(ld_ids, 16)
            nc.vector.tensor_scalar(u_neg[:, :], ids_sb[:, 0, :], 0.0, float(USERS), ALU.is_lt, ALU.mult).then_inc(u_step, 1)
            dve.wait_ge(u_step, 1)
            nc.vector.tensor_tensor(u_wrap[:, :], ids_sb[:, 0, :], u_neg[:, :], ALU.add).then_inc(u_step, 1)
            dve.wait_ge(u_step, 2)
            nc.vector.tensor_scalar(u_row[:, :], u_wrap[:, :], 0.0, float(USERS - 1), ALU.max, ALU.min).then_inc(u_step, 1)
            dve.wait_ge(sizes_set, 13)
            nc.vector.scalar_tensor_tensor(out=s_neg[:, :, :], in0=ids_sb[:, 1:FIELDS, :], scalar=0.0, in1=n_rows[:, :, :],
                                           op0=ALU.is_lt, op1=ALU.mult).then_inc(s_step, 1)
            nc.vector.tensor_tensor(c_col[:, :, :], ids_sb[:, :, :], fm_off[:, :, :], ALU.add).then_inc(c_step, 1)
            dve.wait_ge(s_step, 1)
            nc.vector.tensor_tensor(s_wrap[:, :, :], ids_sb[:, 1:FIELDS, :], s_neg[:, :, :], ALU.add).then_inc(s_step, 1)
            dve.wait_ge(c_step, 1)
            nc.vector.tensor_scalar(c_neg[:, :, :], c_col[:, :, :], 0.0, float(VOCAB), ALU.is_lt, ALU.mult).then_inc(c_step, 1)
            dve.wait_ge(s_step, 2)
            nc.vector.scalar_tensor_tensor(out=s_row[:, :, :], in0=s_wrap[:, :, :], scalar=0.0, in1=last_row[:, :, :],
                                           op0=ALU.max, op1=ALU.min).then_inc(s_step, 1)
            dve.wait_ge(c_step, 2)
            nc.vector.tensor_tensor(c_wrap[:, :, :], c_col[:, :, :], c_neg[:, :, :], ALU.add).then_inc(c_step, 1)
            dve.wait_ge(c_step, 3)
            nc.vector.tensor_scalar(fm_col[:, :, :], c_wrap[:, :, :], 0.0, float(VOCAB - 1), ALU.max, ALU.min).then_inc(c_step, 1)
            dve.wait_ge(ld_scale, 16)
            nc.vector.tensor_copy(scale_h[:, :], scale_sb[:, :]).then_inc(scale_split, 1)
            dve.wait_ge(scale_split, 1)
            nc.vector.tensor_tensor(scale_l[:, :], scale_sb[:, :], scale_h[:, :].bitcast(F32), ALU.subtract).then_inc(scale_split, 1)
            dve.wait_ge(s_step, 3)
            dve.wait_ge(pool_const, 2)
            dve.wait_ge(hot_zero, 1)
            for f, (rows, slot, _) in enumerate(SMALL):
                dst = hot_h if f == 3 else hot
                nc.vector.tensor_tensor(dst[:, :, slot:slot + rows],
                                        row_no[:, 0:rows].unsqueeze(1).to_broadcast([P, T, rows]),
                                        s_row[:, f, :].unsqueeze(2).to_broadcast([P, T, rows]),
                                        ALU.is_equal).then_inc(hot_made, 1)
            dve.wait_ge(hot_made, 4)
            dve.wait_ge(scale_split, 2)
            nc.vector.tensor_tensor(hot_h[:, :, 0:FACE], hot[:, :, :],
                                    scale_h[:, :].bitcast(F32).unsqueeze(2).to_broadcast([P, T, FACE]), ALU.mult).then_inc(hot_scaled, 1)
            nc.vector.tensor_tensor(hot_l[:, :, :], hot[:, :, :],
                                    scale_l[:, :].unsqueeze(2).to_broadcast([P, T, FACE]), ALU.mult).then_inc(hot_scaled, 1)
            nc.vector.memset(hour_ones[:, 0:HOUR0], 0.0).then_inc(ones_set, 1)
            nc.vector.memset(hour_ones[:, HOUR0:SLOTS], 1.0).then_inc(ones_set, 1)
            nc.vector.memset(ones[:, :], 1.0).then_inc(ones_set, 1)
            dve.wait_ge(ones_set, 3)
            nc.vector.tensor_copy(ones_r[:, :], ones[:, :]).then_inc(ones_set, 1)
            dve.wait_ge(ld_b2, 32)
            nc.vector.tensor_copy(b2_r[:, :], b2_sb[:, :]).then_inc(b2_split, 1)
            dve.wait_ge(b2_split, 1)
            nc.vector.tensor_tensor(b2_r[32:33, :], b2_sb[32:33, :], b2_r[32:33, :].bitcast(F32), ALU.subtract).then_inc(b2_split, 1)
            dve.wait_ge(gh_made, 1)
            nc.vector.tensor_tensor(g_l[:, :], p_g[0:SLOTS, :], g_h[:, :].bitcast(F32), ALU.subtract).then_inc(gl_made, 1)
            dve.wait_ge(vish_made, 1)
            nc.vector.scalar_tensor_tensor(out=xa_l[K:P, :], in0=p_vis[K:P, :], scalar=visub_sb[K:P, :],
                                           in1=xa_h[K:P, :].bitcast(F32), op0=ALU.add, op1=ALU.subtract).then_inc(visl_made, 1)
            dve.wait_ge(w1h_made, 1)
            nc.vector.tensor_tensor(w1a_l[:, :], w1a_sb[:, :], w1a_h[:, :].bitcast(F32), ALU.subtract).then_inc(w1l_made, 1)
            for k in range(2):
                dve.wait_ge(w2h_made, k + 1)
                nc.vector.tensor_tensor(w2_l[:, k, :], w2_sb[:, k, :], w2_h[:, k, :].bitcast(F32), ALU.subtract).then_inc(w2l_made, 1)
            dve.wait_ge(userh_made, 1)
            nc.vector.tensor_tensor(xa_l[0:K, :], p_user[0:K, :], xa_h[0:K, :].bitcast(F32), ALU.subtract).then_inc(userl_made, 1)
            dve.wait_ge(fm_done, 1)
            nc.vector.tensor_tensor(esum[:, :, :], user[:, :, :], fm[:, :, 0:K], ALU.add).then_inc(fm_read, 1)
            nc.vector.tensor_tensor(fsq[:, :], scale_sb[:, :], fm[:, :, K + 1], ALU.mult).then_inc(fm_read, 1)
            dve.wait_ge(fm_read, 2)
            nc.vector.tensor_tensor(fsq2[:, :], fsq[:, :], fm[:, :, K], ALU.add).then_inc(fm_read, 1)
            for k in range(2, KT):
                dve.wait_ge(w2h_made, k + 1)
                nc.vector.tensor_tensor(w2_l[:, k, :], w2_sb[:, k, :], w2_h[:, k, :].bitcast(F32), ALU.subtract).then_inc(w2l_made, 1)
            for m in range(KT):
                dve.wait_ge(h1h_made, m + 1)
                nc.vector.scalar_tensor_tensor(out=h1_l[:, m, :], in0=p_h1[m][:, :], scalar=0.0,
                                               in1=h1_h[:, m, :].bitcast(F32), op0=ALU.max, op1=ALU.subtract).then_inc(h1l_made, 1)
            dve.wait_ge(fm_read, 3)
            nc.vector.tensor_tensor(esum2[:, :, :], esum[:, :, :], esum[:, :, :], ALU.mult).then_inc(sumsq, 1)
            nc.vector.tensor_tensor(user2[:, :, :], user[:, :, :], user[:, :, :], ALU.mult).then_inc(sumsq, 1)
            dve.wait_ge(sumsq, 2)
            nc.vector.tensor_tensor(sdiff[:, :, :], esum2[:, :, :], user2[:, :, :], ALU.subtract).then_inc(sumsq, 1)
            dve.wait_ge(sumsq, 3)
            nc.vector.reduce_sum(sred[:, :], sdiff[:, :, :], AX.X).then_inc(sumsq, 1)
            dve.wait_ge(sumsq, 4)
            nc.vector.tensor_tensor(second[:, :], sred[:, :], fsq2[:, :], ALU.subtract).then_inc(sumsq, 1)
            dve.wait_ge(ld_bias, 32)
            nc.vector.tensor_tensor(bias2[:, :], b3_sb[:, :], fmb_sb[:, :], ALU.add).then_inc(sumsq, 1)
            dve.wait_ge(sumsq, 6)
            nc.vector.scalar_tensor_tensor(out=base[:, :, :], in0=second[:, :].unsqueeze(2).to_broadcast([P, T, 2]), scalar=0.5,
                                           in1=bias2[:, :].unsqueeze(1).to_broadcast([P, T, 2]),
                                           op0=ALU.mult, op1=ALU.add).then_inc(base_step, 1)
            dve.wait_ge(ld_w3, 16)
            for t in range(T):
                dve.wait_ge(z_done, t + 1)
                if t >= 2:
                    dve.wait_ge(x3_made, 2 * (t - 1))
                for c in range(2):
                    nc.vector.scalar_tensor_tensor(out=prod[:, t % 2, c, :], in0=p_z[t][:, :], scalar=0.0, in1=w3_sb[:, c, :],
                                                   op0=ALU.max, op1=ALU.mult,
                                                   accum_out=x3[:, t, c:c + 1]).then_inc(x3_made, 1)
            dve.wait_ge(got_fm, 16 * FIELDS * T)
            nc.vector.reduce_sum(lin[:, :, :], fm_rows[:, :, :, :].rearrange("p f t c -> p t c f"), AX.X).then_inc(base_step, 1)
            dve.wait_ge(base_step, 2)
            nc.vector.tensor_tensor(base2[:, :, :], base[:, :, :], lin[:, :, :], ALU.add).then_inc(base_step, 1)
            dve.wait_ge(base_step, 3)
            dve.wait_ge(x3_made, 2 * T)
            nc.vector.tensor_tensor(logit[:, :, :], base2[:, :, :], x3[:, :, :], ALU.add).then_inc(soft, 1)
            dve.wait_ge(soft, 1)
            nc.vector.tensor_tensor(top[:, :], logit[:, :, 0], logit[:, :, 1], ALU.max).then_inc(soft, 1)
            dve.wait_ge(soft, 2)
            nc.vector.tensor_tensor(shifted[:, :, :], logit[:, :, :], top[:, :].unsqueeze(2).to_broadcast([P, T, 2]), ALU.subtract).then_inc(soft, 1)
            dve.wait_ge(exp_made, 1)
            nc.vector.tensor_tensor(esm[:, :], expd[:, :, 0], expd[:, :, 1], ALU.add).then_inc(soft, 1)
            dve.wait_ge(soft, 4)
            nc.vector.reciprocal(rsm[:, :], esm[:, :]).then_inc(soft, 1)
            dve.wait_ge(soft, 5)
            nc.vector.tensor_tensor(prob[:, :, :], expd[:, :, :], rsm[:, :].unsqueeze(2).to_broadcast([P, T, 2]), ALU.mult).then_inc(soft, 1)

        @block.tensor
        def _(pe):
            mm = nc.tensor.matmul
            pe.wait_ge(tabT_tanh, 1)
            pe.wait_ge(ld_w1g, 16)
            mm(p_g[0:SLOTS, :], tabT[:, 0, :], w1g_sb[:, 0, :], start=True, stop=False)
            mm(p_g[0:SLOTS, :], tabT[:, 1, :], w1g_sb[:, 1, :], start=False, stop=False)
            pe.wait_ge(ones_set, 4)
            pe.wait_ge(ld_b1, 16)
            mm(p_g[0:SLOTS, :], hour_ones[:, :], b1_sb[:, :], start=False, stop=True).then_inc(g_done, 1)
            pe.wait_ge(pool_const, 3)
            pe.wait_ge(hot_scaled, 1)
            for t in range(T):
                last = nc.tensor.transpose(p_hot_h[0:SLOTS, t * P:(t + 1) * P], hot_h[:, t, :], ident[:, :])
            last.then_inc(hot_on_slots, 1)
            pe.wait_ge(hot_scaled, 2)
            for t in range(T):
                last = nc.tensor.transpose(p_hot_l[0:FACE, t * P:(t + 1) * P], hot_l[:, t, :], ident[:, :])
            last.then_inc(hot_on_slots, 1)
            pe.wait_ge(ld_visuw, 16)
            pe.wait_ge(ld_vis, 16)
            for v in range(VT):
                last = mm(p_vis[K:P, :], visuw_sb[:, v, :], vis_sb[:, v, :], start=(v == 0), stop=(v == VT - 1))
            last.then_inc(vis_done, 1)
            pe.wait_ge(tab_ready, 2)
            pe.wait_ge(hotT_copied, 2)
            for t in range(T):
                mm(fm[:, t, :], hotT_h[:, t * P:(t + 1) * P].bitcast(F32), tab[:, :], start=True, stop=False)
                last = mm(fm[:, t, :], hotT_l[:, t * P:(t + 1) * P].bitcast(F32), tab[0:FACE, :], start=False, stop=True)
            last.then_inc(fm_done, 1)

            def layer1_tables(m):
                cols = slice(m * P, (m + 1) * P)
                mm(p_h1[m][:, :], g_h[:, cols], hotT_h[:, :], start=True, stop=False)
                mm(p_h1[m][:, :], g_l[:, cols], hotT_h[:, :], start=False, stop=False)
                mm(p_h1[m][:, :], g_h[0:FACE, cols], hotT_l[:, :], start=False, stop=False)

            def layer1_user_visual(m):
                cols = slice(m * P, (m + 1) * P)
                mm(p_h1[m][:, :], w1a_h[:, cols], xa_h[:, :], start=False, stop=False)
                mm(p_h1[m][:, :], w1a_l[:, cols], xa_h[:, :], start=False, stop=False)
                mm(p_h1[m][:, :], w1a_h[:, cols], xa_l[:, :], start=False, stop=True).then_inc(h1_done, 1)

            pe.wait_ge(gh_made, 1)
            pe.wait_ge(gl_made, 1)
            layer1_tables(0)
            for t in range(T):
                pe.wait_ge(got_user[t], 16)
                last = nc.tensor.transpose(p_user[0:K, t * P:(t + 1) * P], user[:, t, :], ident[:, :])
            last.then_inc(user_done, 1)
            pe.wait_ge(visl_made, 1)
            layer1_tables(1)
            layer1_tables(2)
            pe.wait_ge(b2_split, 2)
            pe.wait_ge(fm_read, 3)
            for t in range(T):
                mm(p_z[t][:, :], ones_r[:, :], b2_r[:, :], start=True, stop=False)
            pe.wait_ge(w1l_made, 1)
            pe.wait_ge(userl_made, 1)
            for m in range(3):
                layer1_user_visual(m)
            layer1_tables(3)
            layer1_user_visual(3)

            def layer2(t, ks, last_k):
                rows = slice(t * P, (t + 1) * P)
                for k in ks:
                    mm(p_z[t][:, :], h1_h[:, k, rows], w2_h[:, k, :], start=False, stop=False)
                    mm(p_z[t][:, :], h1_h[:, k, rows], w2_l[:, k, :], start=False, stop=False)
                    last = mm(p_z[t][:, :], h1_l[:, k, rows], w2_h[:, k, :], start=False, stop=(k == last_k))
                return last

            for k in range(KT - 1):
                pe.wait_ge(w2l_made, k + 1)
                pe.wait_ge(h1l_made, k + 1)
                layer2(0, [k], KT - 1)
            layer2(1, range(KT - 1), KT - 1)
            pe.wait_ge(w2l_made, KT)
            pe.wait_ge(h1l_made, KT)
            layer2(0, [KT - 1], KT - 1).then_inc(z_done, 1)
            layer2(1, [KT - 1], KT - 1).then_inc(z_done, 1)
            for t in range(2, T):
                layer2(t, range(KT), KT - 1).then_inc(z_done, 1)


def kernel(**inputs):
    import numpy as np
    import concourse.bacc as bacc
    from concourse.bass_utils import run_bass_kernel_spmd

    def get(name):
        return np.asarray(inputs[name])

    def tiles_first(a, tiles):
        return a.reshape(tiles, P, -1).transpose(1, 0, 2)

    w1T = get("L0_rec_w1").T
    layout = {
        "ids": np.stack([get("r_user_id"), get("r_gender"), get("r_age"), get("r_attribute"), get("r_hour")]
                        ).reshape(FIELDS, P, T).transpose(1, 0, 2),
        "scale": get("r_scale").reshape(P, T),
        "visT": tiles_first(get("r_visual").reshape(P, T, VT * P).transpose(2, 1, 0).reshape(VT * P, BATCH), VT),
        "visuwT": tiles_first(get("L0_rec_visu_w").T, VT),
        "visu_b": get("L0_rec_visu_b").reshape(K, 1),
        "w1a": np.concatenate([w1T[0:K], w1T[5 * K:6 * K]]),
        "w1g": tiles_first(w1T[K:5 * K], 2),
        "w2T": get("L0_rec_w2").T.reshape(KT, P, HID),
        "b1": get("L0_rec_b1").reshape(1, HID),
        "b2": get("L0_rec_b2").reshape(1, HID),
        "w3": get("L0_rec_w3"),
        "b3": get("L0_rec_b3"),
        "fm_b": get("L0_rec_fm_b"),
        "hourT": get("L0_rec_hour_emb").T,
        "genderT": get("L0_rec_gender_emb").T,
        "ageT": get("L0_rec_age_emb").T,
        "attrT": get("L0_rec_attr_emb").T,
        "face_rows": np.concatenate([get("L0_rec_gender_emb"), get("L0_rec_age_emb"), get("L0_rec_attr_emb")]),
        "hour_rows": get("L0_rec_hour_emb"),
        "user_emb": get("L0_rec_user_emb"),
        "fmT": get("L0_rec_fm_w").T,
    }
    nc = bacc.Bacc("TRN2", target_bir_lowering=False, num_devices=1)
    arrays, args = {}, []
    for name, a in layout.items():
        a = np.ascontiguousarray(a)
        arrays[f"{name}_dram"] = a
        args.append(nc.dram_tensor(f"{name}_dram", a.shape, mybir.dt.from_np(a.dtype), kind="ExternalInput").ap())
    out = nc.dram_tensor("out_dram", (P, T, 2), F32, kind="ExternalOutput").ap()
    build_rec(nc, *args, out)
    r = run_bass_kernel_spmd(nc, [arrays], core_ids=[0])
    return r.results[0]["out_dram"].reshape(BATCH, 2)
```

```python
import concourse.bass as bass
from concourse import mybir
from contextlib import ExitStack

F32 = mybir.dt.float32
F32R = mybir.dt.float32r
I32 = mybir.dt.int32
BF16 = mybir.dt.bfloat16
ALU = mybir.AluOpType
ACT = mybir.ActivationFunctionType
AX = mybir.AxisListType

P = 128
BATCH = 512
T = BATCH // P
K = 64
USERS = 125000
GENDER, AGE, ATTR, HOUR = (2, 0, 24), (8, 2, 26), (40, 10, 34), (24, 50, 0)
SMALL = (GENDER, AGE, ATTR, HOUR)
NS = len(SMALL)
FACE = 50
HOT = FACE + 24
HOUR0 = 2 * FACE
SLOTS = HOUR0 + 24
VOCAB = USERS + 24 + 2 + 8 + 40
HID = 512
HALF = HID // 2
KT = HID // P
VT = 256 // P
FMC = K + 2
C_SCALE = 0
C_VISUB = C_SCALE + T
C_TAB = C_VISUB + 1
C_TABT = C_TAB + K
C_VISUW = C_TABT + 2 * SLOTS
C_END = C_VISUW + VT * K
WARM = 8
R_W3 = 0
R_BIAS = R_W3 + 2 * HID
R_FM = R_BIAS + 4
R_END = R_FM + 2 * HOT


def build_rec(nc, ids, params, visT, w1a, w1g, w2T, b12, row, user_emb, fmT, out):
    ctx = ExitStack()
    with ctx:
        def sb(name, shape, dt=F32):
            return ctx.enter_context(nc.sbuf_tensor(name, shape, dt))

        def sem(name):
            return ctx.enter_context(nc.semaphore(name))

        ids_sb = sb("ids_sb", [P, 1 + NS, T], I32)
        params_sb = sb("params_sb", [P, C_END])
        scale_sb = params_sb[:, C_SCALE:C_SCALE + T]
        visub_sb = params_sb[:, C_VISUB:C_VISUB + 1]
        tab_sb = params_sb[0:SLOTS, C_TAB:C_TAB + K]
        tabT_sb = params_sb[:, C_TABT:C_TABT + 2 * SLOTS].rearrange("p (j s) -> p j s", j=2)
        visuw_sb = params_sb[:, C_VISUW:C_VISUW + VT * K].rearrange("p (v k) -> p v k", v=VT)
        vis_sb = sb("vis_sb", [P, VT, BATCH])
        w1a_sb = sb("w1a_sb", [P, HID])
        w1g_sb = sb("w1g_sb", [P, 2, HID])
        w2_sb = sb("w2_sb", [P, KT, HID])
        b12_sb = sb("b12_sb", [33, 2 * HID])
        row_sb = sb("row_sb", [P, R_END])
        w3_sb = row_sb[:, R_W3:R_W3 + 2 * HID].rearrange("p (c n) -> p c n", c=2)
        fmw_sb = row_sb[:, R_FM:R_FM + 2 * HOT].rearrange("p (c s) -> p c s", c=2)
        user = sb("user", [P, T, K])
        fm_user = sb("fm_user", [P, T, 2])
        fm_rare = sb("fm_rare", [P, NS, T, 2])
        ident = sb("ident", [P, P])
        row_no = sb("row_no", [P, 40], I32)
        n_rows = sb("n_rows", [P, NS, T])
        last_row = sb("last_row", [P, NS, T])
        fm_off = sb("fm_off", [P, 1 + NS, T])
        warm = sb("warm", [P, 512], BF16)
        ones = sb("ones", [P, P])
        hour_ones = sb("hour_ones", [33, SLOTS])
        ones_r = sb("ones_r", [33, P], F32R)
        hour_ones_r = sb("hour_ones_r", [33, SLOTS], F32R)
        kind = sb("kind", [SLOTS, 2])
        u_neg = sb("u_neg", [P, T])
        u_wrap = sb("u_wrap", [P, T])
        u_row = sb("u_row", [P, T], I32)
        c_col = sb("c_col", [P, 1 + NS, T])
        c_neg = sb("c_neg", [P, 1 + NS, T])
        c_wrap = sb("c_wrap", [P, 1 + NS, T])
        fm_col = sb("fm_col", [P, 1 + NS, T], I32)
        s_neg = sb("s_neg", [P, NS, T])
        s_wrap = sb("s_wrap", [P, NS, T])
        s_row = sb("s_row", [P, NS, T])
        differs = sb("differs", [P, NS, T])
        outside = sb("outside", [P, 1])
        outside_n = sb("outside_n", [1, 1], I32)
        scale_h = sb("scale_h", [P, T], F32R)
        scale_hl = sb("scale_hl", [P, T, 2])
        hot = sb("hot", [P, T, HOT])
        hot_s = sb("hot_s", [P, T, SLOTS])
        hotT = sb("hotT", [SLOTS, BATCH], F32R)
        tab2 = sb("tab2", [SLOTS, FMC])
        tab_h = sb("tab_h", [SLOTS, FMC], F32R)
        tab_l = sb("tab_l", [SLOTS, FMC], F32R)
        tabT = sb("tabT", [P, 2, SLOTS])
        g_h = sb("g_h", [SLOTS, HID], F32R)
        g_l = sb("g_l", [SLOTS, HID], F32R)
        w1a_h = sb("w1a_h", [P, HID], F32R)
        w1a_l = sb("w1a_l", [P, HID], F32R)
        w2_h = sb("w2_h", [P, KT, HID], F32R)
        w2_l = sb("w2_l", [P, KT, HID], F32R)
        b12_r = sb("b12_r", [33, 2 * HID], F32R)
        xa_h = sb("xa_h", [P, BATCH], F32R)
        xa_l = sb("xa_l", [P, BATCH], F32R)
        h1_h = sb("h1_h", [P, KT, BATCH], F32R)
        h1_l = sb("h1_l", [P, KT, BATCH], F32R)
        sq = sb("sq", [SLOTS, K])
        rowsq = sb("rowsq", [SLOTS, 1])
        small = sb("small", [P, T, FMC])
        esum = sb("esum", [P, T, K])
        esum2 = sb("esum2", [P, T, K])
        user2 = sb("user2", [P, T, K])
        sdiff = sb("sdiff", [P, T, K])
        sred = sb("sred", [P, T])
        fsq = sb("fsq", [P, T])
        fsq2 = sb("fsq2", [P, T])
        second = sb("second", [P, T])
        hot_w = sb("hot_w", [P, 2, T, HOT])
        lin_small = sb("lin_small", [P, T, 2])
        lin = sb("lin", [P, T, 2])
        bias2 = sb("bias2", [P, 2])
        base0 = sb("base0", [P, T, 2])
        base = sb("base", [P, T, 2])
        prod = sb("prod", [P, 2, 2, HID])
        x3 = sb("x3", [P, T, 2])
        x3_half = sb("x3_half", [P, 2])
        base_half = sb("base_half", [P, 2])
        nlogit = sb("nlogit", [P, T, 2])
        ntop = sb("ntop", [P, T])
        expd = sb("expd", [P, T, 2])
        esm = sb("esm", [P, T])
        rsm = sb("rsm", [P, T])
        prob = sb("prob", [P, T, 2])

        bank = [ctx.enter_context(nc.psum_tensor(f"bank{i}", [P, 512], F32)) for i in range(8)]
        p_z = bank[0:4]
        p_small, p_g, p_xa, p_hot = bank[4:8]
        p_h1 = [p_hot, p_g, p_small, p_xa]
        p_z_end = p_hot
        small_ps = p_small[:, 0:T * FMC].rearrange("p (t k) -> p t k", t=T)
        outside_ps = p_small[0:1, T * FMC:T * FMC + 1]

        ld_ids, ld_params, ld_b12 = sem("ld_ids"), sem("ld_params"), sem("ld_b12")
        ld_w1g = [sem(f"ld_w1g{j}") for j in range(2)]
        ld_vis, ld_w1a, ld_row = sem("ld_vis"), sem("ld_w1a"), sem("ld_row")
        ld_w2 = [sem(f"ld_w2_{k}") for k in range(KT)]
        warm_set = sem("warm_set")
        got_user = [sem(f"got_user{t}") for t in range(T)]
        got_fm_user, got_fm_rare, st_out = sem("got_fm_user"), sem("got_fm_rare"), sem("st_out")
        b12_zero, sizes_set, ident_set, rows_set, ones_set, kind_set = (
            sem("b12_zero"), sem("sizes_set"), sem("ident_set"), sem("rows_set"), sem("ones_set"), sem("kind_set"))
        u_step, c_step, s_step, scale_step, hot_step = (
            sem("u_step"), sem("c_step"), sem("s_step"), sem("scale_step"), sem("hot_step"))
        hot_on_slots, hotT_made = sem("hot_on_slots"), sem("hotT_made")
        outside_set, rare_step = sem("outside_set"), sem("rare_step")
        tabT_made, tab_step, tab_split = sem("tabT_made"), sem("tab_step"), sem("tab_split")
        b1_split, b2_split = sem("b1_split"), sem("b2_split")
        g_done, gh_made, gl_made = sem("g_done"), sem("gh_made"), sem("gl_made")
        vis_done, vish_made, visl_made = sem("vis_done"), sem("vish_made"), sem("visl_made")
        user_done, userh_made, userl_made = sem("user_done"), sem("userh_made"), sem("userl_made")
        w1h_made, w1l_made, w2h_made, w2l_made = sem("w1h_made"), sem("w1l_made"), sem("w2h_made"), sem("w2l_made")
        h1_done, h1h_made, h1l_made = sem("h1_done"), sem("h1h_made"), sem("h1l_made")
        small_done, small_read, fsq_step, second_step, lin_step, base_step = (
            sem("small_done"), sem("small_read"), sem("fsq_step"), sem("second_step"), sem("lin_step"), sem("base_step"))
        z_done, x3_made, nlogit_made, ntop_made, exp_made, rsm_made, prob_made = (
            sem("z_done"), sem("x3_made"), sem("nlogit_made"), sem("ntop_made"), sem("exp_made"), sem("rsm_made"),
            sem("prob_made"))

        block = ctx.enter_context(nc.Block())

        @block.sync
        def _(sp):
            sp.dma_start(ids_sb[:, :, :], ids).then_inc(ld_ids, 16)
            sp.dma_start(params_sb[:, :], params).then_inc(ld_params, 16)
            sp.dma_start(w1g_sb[:, 0, :], w1g[0]).then_inc(ld_w1g[0], 16)
            sp.wait_ge(b12_zero, 2)
            sp.dma_start(b12_sb[0:33:32, :], b12).then_inc(ld_b12, 16)
            sp.dma_start(w1g_sb[:, 1, :], w1g[1]).then_inc(ld_w1g[1], 16)
            sp.dma_start(vis_sb[:, :, :], visT).then_inc(ld_vis, 16)
            sp.dma_start(w1a_sb[:, :], w1a).then_inc(ld_w1a, 16)
            for k in range(KT):
                if k == 1:
                    sp.wait_ge(got_user[0], 16)
                sp.dma_start(w2_sb[:, k, :], w2T[k]).then_inc(ld_w2[k], 16)
            sp.dma_start(row_sb[:, :], row.partition_broadcast(P)).then_inc(ld_row, 16)
            sp.wait_ge(prob_made, 2)
            sp.dma_start(out, prob[:, :, :]).then_inc(st_out, 16)
            sp.wait_ge(st_out, 16)

        @block.gpsimd
        def _(pool):
            nc.gpsimd.memset(b12_sb[:, HID:2 * HID], 0.0).then_inc(b12_zero, 1)
            nc.gpsimd.iota(row_no[:, :], [[1, 40]], base=0, channel_multiplier=0).then_inc(rows_set, 1)
            nc.gpsimd.memset(ident[:, :], 0.0).then_inc(ident_set, 1)
            pool.wait_ge(ident_set, 1)
            nc.gpsimd.affine_select(out=ident[:, :], in_=ident[:, :], compare_op=ALU.not_equal, fill=1.0,
                                    base=0, pattern=[[-1, P]], channel_multiplier=1).then_inc(ident_set, 1)
            pool.wait_ge(u_step, 3)
            for t in range(T):
                nc.gpsimd.indirect_dma_start(user[:, t, :], None, user_emb,
                                             bass.IndirectOffsetOnAxis(ap=u_row[:, t:t + 1], axis=0)
                                             ).then_inc(got_user[t], 16)
            pool.wait_ge(c_step, 4)
            for t in range(T):
                nc.gpsimd.indirect_dma_start(fm_user[:, t, :], None, fmT,
                                             bass.IndirectOffsetOnAxis(ap=fm_col[:, 0, t:t + 1], axis=0)
                                             ).then_inc(got_fm_user, 16)
            for t in range(T):
                pool.wait_ge(got_user[t], 16)
            nc.gpsimd.tensor_tensor(user2[:, :, :], user[:, :, :], user[:, :, :], ALU.mult).then_inc(second_step, 1)
            pool.wait_ge(small_read, 1)
            nc.gpsimd.tensor_tensor(esum[:, :, :], user[:, :, :], small[:, :, 0:K], ALU.add).then_inc(second_step, 1)
            pool.wait_ge(second_step, 2)
            nc.gpsimd.tensor_tensor(esum2[:, :, :], esum[:, :, :], esum[:, :, :], ALU.mult).then_inc(second_step, 1)
            pool.wait_ge(second_step, 3)
            nc.gpsimd.tensor_tensor(sdiff[:, :, :], esum2[:, :, :], user2[:, :, :], ALU.subtract).then_inc(second_step, 1)
            pool.wait_ge(ld_row, 16)
            pool.wait_ge(hot_step, 4)
            for c in range(2):
                nc.gpsimd.tensor_tensor(hot_w[:, c, :, :], hot[:, :, :],
                                        fmw_sb[:, c, :].unsqueeze(1).to_broadcast([P, T, HOT]),
                                        ALU.mult).then_inc(lin_step, 1)
            pool.wait_ge(lin_step, 3)
            pool.wait_ge(outside_set, 1)
            n_outside = nc.gpsimd.value_load(outside_n[0:1, 0:1], min_val=0, max_val=NS * BATCH)
            with nc.gpsimd.If(n_outside > 0):
                for f in range(NS):
                    for t in range(T):
                        nc.gpsimd.indirect_dma_start(fm_rare[:, f, t, :], None, fmT,
                                                     bass.IndirectOffsetOnAxis(ap=fm_col[:, 1 + f, t:t + 1], axis=0)
                                                     ).then_inc(got_fm_rare, 16)
                pool.wait_ge(got_fm_rare, 16 * NS * T)
                nc.gpsimd.tensor_tensor(fm_rare[:, 0:2, :, :], fm_rare[:, 0:2, :, :], fm_rare[:, 2:4, :, :],
                                        ALU.add).then_inc(rare_step, 1)
                pool.wait_ge(rare_step, 1)
                nc.gpsimd.tensor_tensor(lin_small[:, :, :], fm_rare[:, 0, :, :], fm_rare[:, 1, :, :],
                                        ALU.add).then_inc(rare_step, 1)
                pool.wait_ge(rare_step, 2)
            pool.wait_ge(got_fm_user, 16 * T)
            nc.gpsimd.tensor_tensor(lin[:, :, :], lin_small[:, :, :], fm_user[:, :, :], ALU.add).then_inc(lin_step, 1)

        @block.scalar
        def _(act):
            act.wait_ge(ld_params, 16)
            nc.scalar.activation(tabT[:, :, 0:HOUR0], tabT_sb[:, :, 0:HOUR0], ACT.Tanh).then_inc(tabT_made, 1)
            nc.scalar.activation(tabT[:, :, HOUR0:SLOTS], tabT_sb[:, :, HOUR0:SLOTS], ACT.Copy).then_inc(tabT_made, 1)
            nc.scalar.activation(tab2[:, 0:K], tab_sb, ACT.Copy).then_inc(tab_step, 1)
            act.wait_ge(tab_step, 1)
            nc.scalar.activation(tab2[0:HOUR0, 0:K], tab_sb[0:HOUR0, :], ACT.Tanh).then_inc(tab_step, 1)
            act.wait_ge(ld_b12, 16)
            nc.scalar.activation(b12_r[:, 0:HID], b12_sb[:, 0:HID], ACT.Copy).then_inc(b1_split, 1)
            act.wait_ge(tab_step, 2)
            nc.scalar.activation(sq[:, :], tab2[:, 0:K], ACT.Square, accum_out=rowsq[:, :]).then_inc(tab_step, 1)
            nc.scalar.activation(b12_r[:, HID:2 * HID], b12_sb[:, HID:2 * HID], ACT.Copy).then_inc(b2_split, 1)
            act.wait_ge(hot_on_slots, 1)
            nc.scalar.activation(hotT[:, :], p_hot[0:SLOTS, :], ACT.Copy).then_inc(hotT_made, 1)
            act.wait_ge(tab_step, 4)
            nc.scalar.activation(tab_h[:, :], tab2[:, :], ACT.Copy).then_inc(tab_split, 1)
            act.wait_ge(vis_done, 1)
            nc.scalar.activation(xa_h[K:P, :], p_xa[K:P, :], ACT.Identity, bias=visub_sb[K:P, :]).then_inc(vish_made, 1)
            act.wait_ge(ld_w1a, 16)
            nc.scalar.activation(w1a_h[:, :], w1a_sb[:, :], ACT.Copy).then_inc(w1h_made, 1)
            act.wait_ge(g_done, 1)
            nc.scalar.activation(g_h[:, :], p_g[0:SLOTS, :], ACT.Copy).then_inc(gh_made, 1)
            act.wait_ge(small_done, 1)
            nc.scalar.activation(small[:, :, :], small_ps, ACT.Copy).then_inc(small_read, 1)
            nc.scalar.activation(outside_n[:, :], outside_ps, ACT.Copy).then_inc(outside_set, 1)

            def w2_high(k):
                act.wait_ge(ld_w2[k], 16)
                nc.scalar.activation(w2_h[:, k, :], w2_sb[:, k, :], ACT.Copy).then_inc(w2h_made, 1)

            act.wait_ge(user_done, 1)
            nc.scalar.activation(xa_h[0:K, :], p_xa[0:K, :], ACT.Copy).then_inc(userh_made, 1)
            for k in range(KT):
                w2_high(k)
            for m in range(KT):
                act.wait_ge(h1_done, m + 1)
                nc.scalar.activation(h1_h[:, m, :], p_h1[m][:, :], ACT.Relu).then_inc(h1h_made, 1)
            for t in range(T):
                act.wait_ge(ntop_made, max(t, 1))
                nc.scalar.activation(expd[:, t, :], nlogit[:, t, :], ACT.Exp, scale=-1.0, bias=ntop[:, t:t + 1],
                                     accum_out=esm[:, t:t + 1]).then_inc(exp_made, 1)

        @block.vector
        def _(dve):
            nc.vector.memset(warm[:, :], 0.0).then_inc(warm_set, 1)
            nc.vector.memset(b12_sb[:, 0:HID], 0.0).then_inc(b12_zero, 1)
            for f, (rows, _, col) in enumerate(SMALL):
                nc.vector.memset(n_rows[:, f, :], float(rows)).then_inc(sizes_set, 1)
                nc.vector.memset(last_row[:, f, :], float(rows - 1)).then_inc(sizes_set, 1)
                nc.vector.memset(fm_off[:, 1 + f, :], float(USERS + col)).then_inc(sizes_set, 1)
            nc.vector.memset(fm_off[:, 0, :], 0.0).then_inc(sizes_set, 1)
            nc.vector.memset(ones[:, :], 1.0).then_inc(ones_set, 1)
            nc.vector.memset(hour_ones[:, 0:HOUR0], 0.0).then_inc(ones_set, 1)
            nc.vector.memset(hour_ones[:, HOUR0:SLOTS], 1.0).then_inc(ones_set, 1)
            dve.wait_ge(ones_set, 3)
            nc.vector.tensor_copy(ones_r[:, :], ones[0:33, :]).then_inc(ones_set, 1)
            nc.vector.tensor_copy(hour_ones_r[:, :], hour_ones[:, :]).then_inc(ones_set, 1)
            dve.wait_ge(ld_ids, 16)
            nc.vector.tensor_scalar(u_neg[:, :], ids_sb[:, 0, :], 0.0, float(USERS), ALU.is_lt, ALU.mult).then_inc(u_step, 1)
            dve.wait_ge(u_step, 1)
            nc.vector.tensor_tensor(u_wrap[:, :], ids_sb[:, 0, :], u_neg[:, :], ALU.add).then_inc(u_step, 1)
            dve.wait_ge(u_step, 2)
            nc.vector.tensor_scalar(u_row[:, :], u_wrap[:, :], 0.0, float(USERS - 1), ALU.max, ALU.min).then_inc(u_step, 1)
            dve.wait_ge(sizes_set, 3 * NS + 1)
            nc.vector.scalar_tensor_tensor(out=s_neg[:, :, :], in0=ids_sb[:, 1:1 + NS, :], scalar=0.0, in1=n_rows[:, :, :],
                                           op0=ALU.is_lt, op1=ALU.mult).then_inc(s_step, 1)
            nc.vector.tensor_tensor(c_col[:, :, :], ids_sb[:, :, :], fm_off[:, :, :], ALU.add).then_inc(c_step, 1)
            dve.wait_ge(s_step, 1)
            nc.vector.tensor_tensor(s_wrap[:, :, :], ids_sb[:, 1:1 + NS, :], s_neg[:, :, :], ALU.add).then_inc(s_step, 1)
            dve.wait_ge(c_step, 1)
            nc.vector.tensor_scalar(c_neg[:, :, :], c_col[:, :, :], 0.0, float(VOCAB), ALU.is_lt, ALU.mult).then_inc(c_step, 1)
            dve.wait_ge(s_step, 2)
            nc.vector.scalar_tensor_tensor(out=s_row[:, :, :], in0=s_wrap[:, :, :], scalar=0.0, in1=last_row[:, :, :],
                                           op0=ALU.max, op1=ALU.min).then_inc(s_step, 1)
            dve.wait_ge(c_step, 2)
            nc.vector.tensor_tensor(c_wrap[:, :, :], c_col[:, :, :], c_neg[:, :, :], ALU.add).then_inc(c_step, 1)
            dve.wait_ge(c_step, 3)
            nc.vector.tensor_scalar(fm_col[:, :, :], c_wrap[:, :, :], 0.0, float(VOCAB - 1), ALU.max, ALU.min).then_inc(c_step, 1)
            dve.wait_ge(s_step, 3)
            dve.wait_ge(rows_set, 1)
            for f, (rows, place, _) in enumerate(SMALL):
                nc.vector.tensor_tensor(hot[:, :, place:place + rows],
                                        row_no[:, 0:rows].unsqueeze(1).to_broadcast([P, T, rows]),
                                        s_row[:, f, :].unsqueeze(2).to_broadcast([P, T, rows]),
                                        ALU.is_equal).then_inc(hot_step, 1)
            dve.wait_ge(ld_params, 16)
            nc.vector.tensor_copy(scale_h[:, :], scale_sb).then_inc(scale_step, 1)
            dve.wait_ge(scale_step, 1)
            nc.vector.tensor_copy(scale_hl[:, :, 0], scale_h[:, :].bitcast(F32)).then_inc(scale_step, 1)
            nc.vector.tensor_tensor(scale_hl[:, :, 1], scale_sb, scale_h[:, :].bitcast(F32), ALU.subtract).then_inc(scale_step, 1)
            dve.wait_ge(hot_step, 4)
            dve.wait_ge(scale_step, 3)
            nc.vector.tensor_tensor(hot_s[:, :, 0:HOUR0].rearrange("p t (j s) -> p t j s", j=2),
                                    hot[:, :, 0:FACE].unsqueeze(2).to_broadcast([P, T, 2, FACE]),
                                    scale_hl[:, :, :].unsqueeze(3).to_broadcast([P, T, 2, FACE]),
                                    ALU.mult).then_inc(hot_step, 1)
            nc.vector.tensor_copy(hot_s[:, :, HOUR0:SLOTS], hot[:, :, FACE:HOT]).then_inc(hot_step, 1)
            nc.vector.scalar_tensor_tensor(out=differs[:, :, :], in0=s_row[:, :, :], scalar=0.0, in1=ids_sb[:, 1:1 + NS, :],
                                           op0=ALU.add, op1=ALU.not_equal, accum_out=outside[:, :]).then_inc(s_step, 1)
            dve.wait_ge(b1_split, 1)
            nc.vector.tensor_tensor(b12_r[32:33, 0:HID], b12_sb[32:33, 0:HID], b12_r[32:33, 0:HID].bitcast(F32),
                                    ALU.subtract).then_inc(b1_split, 1)
            nc.vector.memset(kind[:, 0:1], 0.0).then_inc(kind_set, 1)
            nc.vector.memset(kind[:, 1:2], 1.0).then_inc(kind_set, 1)
            dve.wait_ge(kind_set, 2)
            nc.vector.memset(kind[96:SLOTS, 0:1], 1.0).then_inc(kind_set, 1)
            nc.vector.memset(kind[96:SLOTS, 1:2], 0.0).then_inc(kind_set, 1)
            dve.wait_ge(kind_set, 4)
            nc.vector.memset(kind[96:HOUR0, 0:1], 0.0).then_inc(kind_set, 1)
            nc.vector.memset(kind[96:HOUR0, 1:2], 1.0).then_inc(kind_set, 1)
            dve.wait_ge(kind_set, 6)
            dve.wait_ge(tab_step, 3)
            nc.vector.tensor_scalar(tab2[:, K:FMC], kind[:, :], rowsq[:, :], None, ALU.mult).then_inc(tab_step, 1)
            dve.wait_ge(b2_split, 1)
            nc.vector.tensor_tensor(b12_r[32:33, HID:2 * HID], b12_sb[32:33, HID:2 * HID],
                                    b12_r[32:33, HID:2 * HID].bitcast(F32), ALU.subtract).then_inc(b2_split, 1)
            dve.wait_ge(tab_split, 1)
            nc.vector.tensor_tensor(tab_l[:, :], tab2[:, :], tab_h[:, :].bitcast(F32), ALU.subtract).then_inc(tab_split, 1)
            dve.wait_ge(vish_made, 1)
            nc.vector.scalar_tensor_tensor(out=xa_l[K:P, :], in0=p_xa[K:P, :], scalar=visub_sb[K:P, :],
                                           in1=xa_h[K:P, :].bitcast(F32), op0=ALU.add, op1=ALU.subtract).then_inc(visl_made, 1)
            dve.wait_ge(w1h_made, 1)
            nc.vector.tensor_tensor(w1a_l[:, :], w1a_sb[:, :], w1a_h[:, :].bitcast(F32), ALU.subtract).then_inc(w1l_made, 1)
            dve.wait_ge(gh_made, 1)
            nc.vector.tensor_tensor(g_l[:, :], p_g[0:SLOTS, :], g_h[:, :].bitcast(F32), ALU.subtract).then_inc(gl_made, 1)
            def w2_low(k):
                dve.wait_ge(w2h_made, k + 1)
                nc.vector.tensor_tensor(w2_l[:, k, :], w2_sb[:, k, :], w2_h[:, k, :].bitcast(F32), ALU.subtract).then_inc(w2l_made, 1)

            dve.wait_ge(userh_made, 1)
            nc.vector.tensor_tensor(xa_l[0:K, :], p_xa[0:K, :], xa_h[0:K, :].bitcast(F32), ALU.subtract).then_inc(userl_made, 1)
            for k in range(KT):
                w2_low(k)

            for m in range(KT):
                dve.wait_ge(h1h_made, m + 1)
                nc.vector.scalar_tensor_tensor(out=h1_l[:, m, :], in0=p_h1[m][:, :], scalar=0.0,
                                               in1=h1_h[:, m, :].bitcast(F32),
                                               op0=ALU.max, op1=ALU.subtract).then_inc(h1l_made, 1)
            dve.wait_ge(lin_step, 2)
            nc.vector.reduce_sum(lin_small[:, :, :], hot_w[:, :, :, :].rearrange("p c t s -> p t c s"), AX.X).then_inc(lin_step, 1)
            dve.wait_ge(small_read, 1)
            nc.vector.tensor_tensor(fsq[:, :], scale_sb, small[:, :, K + 1], ALU.mult).then_inc(fsq_step, 1)
            dve.wait_ge(fsq_step, 1)
            nc.vector.tensor_tensor(fsq2[:, :], fsq[:, :], small[:, :, K], ALU.add).then_inc(fsq_step, 1)
            dve.wait_ge(second_step, 4)
            nc.vector.reduce_sum(sred[:, :], sdiff[:, :, :], AX.X).then_inc(second_step, 1)
            nc.vector.tensor_tensor(bias2[:, :], row_sb[:, R_BIAS:R_BIAS + 2], row_sb[:, R_BIAS + 2:R_BIAS + 4],
                                    ALU.add).then_inc(base_step, 1)
            dve.wait_ge(second_step, 5)
            dve.wait_ge(fsq_step, 2)
            nc.vector.tensor_tensor(second[:, :], sred[:, :], fsq2[:, :], ALU.subtract).then_inc(second_step, 1)
            dve.wait_ge(second_step, 6)
            dve.wait_ge(base_step, 1)
            nc.vector.scalar_tensor_tensor(out=base0[:, :, :], in0=second[:, :].unsqueeze(2).to_broadcast([P, T, 2]), scalar=0.5,
                                           in1=bias2[:, :].unsqueeze(1).to_broadcast([P, T, 2]),
                                           op0=ALU.mult, op1=ALU.add).then_inc(base_step, 1)

            def layer3(z, t, c, cols, total):
                nc.vector.scalar_tensor_tensor(out=prod[:, t % 2, c, cols], in0=z, scalar=0.0,
                                               in1=w3_sb[:, c, cols], op0=ALU.max, op1=ALU.mult,
                                               accum_out=total).then_inc(x3_made, 1)

            def softmax_top(ts, x, rest, step):
                nc.vector.scalar_tensor_tensor(out=nlogit[:, ts, :], in0=x, scalar=-1.0, in1=rest,
                                               op0=ALU.mult, op1=ALU.subtract).then_inc(nlogit_made, 1)
                dve.wait_ge(nlogit_made, step)
                nc.vector.tensor_tensor(ntop[:, ts], nlogit[:, ts, 0], nlogit[:, ts, 1], ALU.min).then_inc(ntop_made, 1)

            def softmax_divide(ts, step):
                nc.vector.reciprocal(rsm[:, ts], esm[:, ts]).then_inc(rsm_made, 1)
                dve.wait_ge(rsm_made, step)
                nc.vector.tensor_tensor(prob[:, ts, :], expd[:, ts, :],
                                        rsm[:, ts].unsqueeze(2).to_broadcast([P, ts.stop - ts.start, 2]),
                                        ALU.mult).then_inc(prob_made, 1)

            for t in range(2):
                dve.wait_ge(z_done, t + 1)
                for c in range(2):
                    layer3(p_z[t][:, :], t, c, slice(0, HID), x3[:, t, c:c + 1])
            dve.wait_ge(base_step, 2)
            dve.wait_ge(lin_step, 4)
            nc.vector.tensor_tensor(base[:, :, :], base0[:, :, :], lin[:, :, :], ALU.add).then_inc(base_step, 1)
            dve.wait_ge(base_step, 3)
            dve.wait_ge(x3_made, 4)
            softmax_top(slice(0, 2), x3[:, 0:2, :], base[:, 0:2, :], 1)
            dve.wait_ge(z_done, 3)
            for c in range(2):
                layer3(p_z[2][:, :], 2, c, slice(0, HID), x3[:, 2, c:c + 1])
            dve.wait_ge(z_done, 4)
            for c in range(2):
                layer3(p_z[3][:, 0:HALF], 3, c, slice(0, HALF), x3_half[:, c:c + 1])
            dve.wait_ge(x3_made, 8)
            softmax_top(slice(2, 3), x3[:, 2:3, :], base[:, 2:3, :], 2)
            nc.vector.tensor_tensor(base_half[:, :], base[:, 3, :], x3_half[:, :], ALU.add).then_inc(base_step, 1)
            dve.wait_ge(base_step, 4)
            dve.wait_ge(z_done, 5)
            for c in range(2):
                layer3(p_z_end[:, 0:HALF], 3, c, slice(HALF, HID), x3[:, 3, c:c + 1])
            dve.wait_ge(x3_made, 10)
            softmax_top(slice(3, 4), x3[:, 3:4, :], base_half[:, :].unsqueeze(1), 3)
            dve.wait_ge(exp_made, 3)
            softmax_divide(slice(0, 3), 1)
            dve.wait_ge(exp_made, 4)
            softmax_divide(slice(3, 4), 2)

        @block.tensor
        def _(pe):
            mm = nc.tensor.matmul
            pe.wait_ge(warm_set, 1)
            for _ in range(WARM):
                mm(p_z[0][:, :], warm[:, 0:P], warm[:, :], start=True, stop=True)
            pe.wait_ge(tabT_made, 2)
            pe.wait_ge(ld_w1g[0], 16)
            mm(p_g[0:SLOTS, :], tabT[:, 0, :], w1g_sb[:, 0, :], start=True, stop=False)
            pe.wait_ge(ident_set, 2)
            pe.wait_ge(hot_step, 6)
            for t in range(T):
                last = nc.tensor.transpose(p_hot[0:SLOTS, t * P:(t + 1) * P], hot_s[:, t, :], ident[:, :])
            last.then_inc(hot_on_slots, 1)
            pe.wait_ge(ld_vis, 16)
            for v in range(VT):
                last = mm(p_xa[K:P, :], visuw_sb[:, v, :], vis_sb[:, v, :], start=(v == 0), stop=(v == VT - 1))
            last.then_inc(vis_done, 1)
            pe.wait_ge(ld_w1g[1], 16)
            mm(p_g[0:SLOTS, :], tabT[:, 1, :], w1g_sb[:, 1, :], start=False, stop=False)
            pe.wait_ge(ones_set, 5)
            pe.wait_ge(b1_split, 2)
            mm(p_g[0:SLOTS, :], hour_ones_r[:, :], b12_r[:, 0:HID], start=False, stop=True).then_inc(g_done, 1)
            pe.wait_ge(s_step, 4)
            mm(outside_ps, outside[:, :], ones[:, 0:1], start=True, stop=True)
            pe.wait_ge(tab_split, 2)
            pe.wait_ge(hotT_made, 1)
            for t in range(T):
                mm(small_ps[:, t, :], hotT[:, t * P:(t + 1) * P], tab_h[:, :], start=True, stop=False)
                last = mm(small_ps[:, t, :], hotT[:, t * P:(t + 1) * P], tab_l[:, :], start=False, stop=True)
            last.then_inc(small_done, 1)

            def layer1_tables(m):
                cols = slice(m * P, (m + 1) * P)
                mm(p_h1[m][:, :], g_h[:, cols], hotT[:, :], start=True, stop=False)
                mm(p_h1[m][:, :], g_l[:, cols], hotT[:, :], start=False, stop=False)

            def layer1_user_visual(m):
                cols = slice(m * P, (m + 1) * P)
                mm(p_h1[m][:, :], w1a_h[:, cols], xa_h[:, :], start=False, stop=False)
                mm(p_h1[m][:, :], w1a_l[:, cols], xa_h[:, :], start=False, stop=False)
                mm(p_h1[m][:, :], w1a_h[:, cols], xa_l[:, :], start=False, stop=True).then_inc(h1_done, 1)

            pe.wait_ge(visl_made, 1)
            for t in range(T):
                pe.wait_ge(got_user[t], 16)
                last = nc.tensor.transpose(p_xa[0:K, t * P:(t + 1) * P], user[:, t, :], ident[:, :])
            last.then_inc(user_done, 1)
            pe.wait_ge(b2_split, 2)
            for t in range(T):
                cols = HID if t < T - 1 else HALF
                mm(p_z[t][:, 0:cols], ones_r[:, :], b12_r[:, HID:HID + cols], start=True, stop=False)
            pe.wait_ge(gl_made, 1)
            layer1_tables(0)
            layer1_tables(1)
            pe.wait_ge(outside_set, 1)
            layer1_tables(2)
            pe.wait_ge(w1l_made, 1)
            pe.wait_ge(userl_made, 1)
            for m in range(KT - 1):
                layer1_user_visual(m)
            layer1_tables(KT - 1)
            layer1_user_visual(KT - 1)

            def layer2(z, t, k, cols=slice(0, HID)):
                rows = slice(t * P, (t + 1) * P)
                mm(z, h1_h[:, k, rows], w2_h[:, k, cols], start=False, stop=False)
                mm(z, h1_h[:, k, rows], w2_l[:, k, cols], start=False, stop=False)
                return mm(z, h1_l[:, k, rows], w2_h[:, k, cols], start=False, stop=(k == KT - 1))

            for k in range(KT - 1):
                pe.wait_ge(w2l_made, k + 1)
                pe.wait_ge(h1l_made, k + 1)
                layer2(p_z[0][:, :], 0, k)
            for k in range(KT - 1):
                layer2(p_z[1][:, :], 1, k)
            mm(p_z_end[:, 0:HALF], ones_r[:, :], b12_r[:, HID + HALF:2 * HID], start=True, stop=False)
            pe.wait_ge(w2l_made, KT)
            pe.wait_ge(h1l_made, KT)
            layer2(p_z[0][:, :], 0, KT - 1).then_inc(z_done, 1)
            layer2(p_z[1][:, :], 1, KT - 1).then_inc(z_done, 1)
            for k in range(KT):
                last = layer2(p_z[2][:, :], 2, k)
            last.then_inc(z_done, 1)
            for z, h in ((p_z[3], 0), (p_z_end, 1)):
                for k in range(KT):
                    last = layer2(z[:, 0:HALF], 3, k, slice(h * HALF, (h + 1) * HALF))
                last.then_inc(z_done, 1)


def kernel(**inputs):
    import numpy as np
    import concourse.bacc as bacc
    from concourse.bass_utils import run_bass_kernel_spmd

    def get(name):
        return np.asarray(inputs[name])

    def tiles_inside(a, tiles):
        return a.reshape(tiles, P, -1).transpose(1, 0, 2)

    user, gender, age, attr, hour = (get(f"r_{n}") for n in ("user_id", "gender", "age", "attribute", "hour"))
    gender_e, age_e, attr_e, hour_e = (get(f"L0_rec_{n}_emb") for n in ("gender", "age", "attr", "hour"))
    w1T = get("L0_rec_w1").T
    fm_w = get("L0_rec_fm_w")

    params = np.zeros((P, C_END), np.float32)
    params[:, C_SCALE:C_SCALE + T] = get("r_scale").reshape(P, T)
    params[K:P, C_VISUB] = get("L0_rec_visu_b")
    params[0:SLOTS, C_TAB:C_TAB + K] = np.concatenate([gender_e, age_e, attr_e] * 2 + [hour_e])
    tabT = params[:, C_TABT:C_TABT + 2 * SLOTS].reshape(P, 2, SLOTS)
    tabT[0:K, 0, HOUR0:SLOTS] = hour_e.T
    for s in (0, FACE):
        tabT[K:P, 0, s:s + 2] = gender_e.T
        tabT[K:P, 1, s + 2:s + 10] = age_e.T
        tabT[0:K, 1, s + 10:s + FACE] = attr_e.T
    params[:, C_TABT:C_TABT + 2 * SLOTS] = tabT.reshape(P, 2 * SLOTS)
    params[:, C_VISUW:C_END] = tiles_inside(get("L0_rec_visu_w").T, VT).reshape(P, VT * K)

    row = np.concatenate([get("L0_rec_w3").reshape(-1), get("L0_rec_b3"), get("L0_rec_fm_b")]
                         + [fm_w[c, USERS + col:USERS + col + rows] for c in range(2) for rows, _, col in SMALL])
    layout = {
        "ids": np.stack([user, gender, age, attr, hour]).reshape(1 + NS, P, T).transpose(1, 0, 2),
        "params": params,
        "visT": tiles_inside(get("r_visual").reshape(P, T, VT * P).transpose(2, 1, 0).reshape(VT * P, BATCH), VT),
        "w1a": np.concatenate([w1T[0:K], w1T[5 * K:6 * K]]),
        "w1g": w1T[K:5 * K].reshape(2, P, HID),
        "w2T": get("L0_rec_w2").T.reshape(KT, P, HID),
        "b12": np.stack([np.concatenate([get("L0_rec_b1"), get("L0_rec_b2")])] * 2),
        "row": row,
        "user_emb": get("L0_rec_user_emb"),
        "fmT": fm_w.T,
    }
    nc = bacc.Bacc("TRN2", target_bir_lowering=False, num_devices=1)
    arrays, args = {}, []
    for name, a in layout.items():
        a = np.ascontiguousarray(a)
        arrays[f"{name}_dram"] = a
        args.append(nc.dram_tensor(f"{name}_dram", a.shape, mybir.dt.from_np(a.dtype), kind="ExternalInput").ap())
    out = nc.dram_tensor("out_dram", (P, T, 2), F32, kind="ExternalOutput").ap()
    build_rec(nc, *args, out)
    r = run_bass_kernel_spmd(nc, [arrays], core_ids=[0])
    return r.results[0]["out_dram"].reshape(BATCH, 2)
```
